# Optimizing a Trainium2 kernel written in Bass

```python
import numpy as np
import jax
import jax.numpy as jnp

def _softmax(x, axis=-1):
    return jax.nn.softmax(x, axis=axis)

def _gelu(x):
    return jax.nn.gelu(x, approximate=True)

def _silu(x):
    return jax.nn.silu(x)

def _sigmoid(x):
    return jax.nn.sigmoid(x)

def _layernorm(x, axis=-1, eps=1e-05):
    m = jnp.mean(x, axis=axis, keepdims=True)
    v = jnp.var(x, axis=axis, keepdims=True)
    return (x - m) / jnp.sqrt(v + eps)

def _scatter_add(tgt, idx, src, axis=0):
    return tgt.at[idx].add(src)

def _segment_sum(src, seg, n):
    return jax.ops.segment_sum(src, seg, n)
kernel_name = 'mk_dlrm_tower_d1_rec_r8_c0591b'

def setup_inputs(seed: int=0):
    np.random.seed(seed)
    _w = jnp.asarray

    def _rec_inputs():
        import jax
        import jax.numpy as jnp
        _tk = jax.random.key(seed)
        ids = jnp.stack([jax.random.randint(jax.random.fold_in(_tk, 200 + f), (512,), 0, v, jnp.int32) for f, v in enumerate([125000, 1000, 1000, 12500, 1000, 1000, 12500, 1250, 12500, 12500, 12500, 1000, 1250, 1000, 1000, 12500, 1000, 12500, 1250, 12500, 12500, 1250, 1000, 1000, 1000, 1000])], axis=1)
        tbl_0 = 0.05 * jax.random.normal(jax.random.fold_in(_tk, 500 + 0), (125000, 128), jnp.float32)
        tbl_1 = 0.05 * jax.random.normal(jax.random.fold_in(_tk, 500 + 1), (1000, 128), jnp.float32)
        tbl_2 = 0.05 * jax.random.normal(jax.random.fold_in(_tk, 500 + 2), (1000, 128), jnp.float32)
        tbl_3 = 0.05 * jax.random.normal(jax.random.fold_in(_tk, 500 + 3), (12500, 128), jnp.float32)
        tbl_4 = 0.05 * jax.random.normal(jax.random.fold_in(_tk, 500 + 4), (1000, 128), jnp.float32)
        tbl_5 = 0.05 * jax.random.normal(jax.random.fold_in(_tk, 500 + 5), (1000, 128), jnp.float32)
        tbl_6 = 0.05 * jax.random.normal(jax.random.fold_in(_tk, 500 + 6), (12500, 128), jnp.float32)
        tbl_7 = 0.05 * jax.random.normal(jax.random.fold_in(_tk, 500 + 7), (1250, 128), jnp.float32)
        tbl_8 = 0.05 * jax.random.normal(jax.random.fold_in(_tk, 500 + 8), (12500, 128), jnp.float32)
        tbl_9 = 0.05 * jax.random.normal(jax.random.fold_in(_tk, 500 + 9), (12500, 128), jnp.float32)
        tbl_10 = 0.05 * jax.random.normal(jax.random.fold_in(_tk, 500 + 10), (12500, 128), jnp.float32)
        tbl_11 = 0.05 * jax.random.normal(jax.random.fold_in(_tk, 500 + 11), (1000, 128), jnp.float32)
        tbl_12 = 0.05 * jax.random.normal(jax.random.fold_in(_tk, 500 + 12), (1250, 128), jnp.float32)
        tbl_13 = 0.05 * jax.random.normal(jax.random.fold_in(_tk, 500 + 13), (1000, 128), jnp.float32)
        tbl_14 = 0.05 * jax.random.normal(jax.random.fold_in(_tk, 500 + 14), (1000, 128), jnp.float32)
        tbl_15 = 0.05 * jax.random.normal(jax.random.fold_in(_tk, 500 + 15), (12500, 128), jnp.float32)
        tbl_16 = 0.05 * jax.random.normal(jax.random.fold_in(_tk, 500 + 16), (1000, 128), jnp.float32)
        tbl_17 = 0.05 * jax.random.normal(jax.random.fold_in(_tk, 500 + 17), (12500, 128), jnp.float32)
        tbl_18 = 0.05 * jax.random.normal(jax.random.fold_in(_tk, 500 + 18), (1250, 128), jnp.float32)
        tbl_19 = 0.05 * jax.random.normal(jax.random.fold_in(_tk, 500 + 19), (12500, 128), jnp.float32)
        tbl_20 = 0.05 * jax.random.normal(jax.random.fold_in(_tk, 500 + 20), (12500, 128), jnp.float32)
        tbl_21 = 0.05 * jax.random.normal(jax.random.fold_in(_tk, 500 + 21), (1250, 128), jnp.float32)
        tbl_22 = 0.05 * jax.random.normal(jax.random.fold_in(_tk, 500 + 22), (1000, 128), jnp.float32)
        tbl_23 = 0.05 * jax.random.normal(jax.random.fold_in(_tk, 500 + 23), (1000, 128), jnp.float32)
        tbl_24 = 0.05 * jax.random.normal(jax.random.fold_in(_tk, 500 + 24), (1000, 128), jnp.float32)
        tbl_25 = 0.05 * jax.random.normal(jax.random.fold_in(_tk, 500 + 25), (1000, 128), jnp.float32)
        _rk = jax.random.fold_in(_tk, 7)
        r_bottom_output = -0.000520686 + 1.00062 * jax.random.normal(jax.random.fold_in(_rk, 101), (512, 128), jnp.float32)
        W_top1 = 0.0456912 * jax.random.normal(jax.random.fold_in(_tk, 801), (479, 512), jnp.float32)
        W_top2 = 0.0441942 * jax.random.normal(jax.random.fold_in(_tk, 802), (512, 256), jnp.float32)
        W_top3 = 0.0625 * jax.random.normal(jax.random.fold_in(_tk, 803), (256, 1), jnp.float32)
        b_top1 = jnp.zeros((512,), jnp.float32)
        b_top2 = jnp.zeros((256,), jnp.float32)
        return (r_bottom_output, ids, tbl_0, tbl_1, tbl_2, tbl_3, tbl_4, tbl_5, tbl_6, tbl_7, tbl_8, tbl_9, tbl_10, tbl_11, tbl_12, tbl_13, tbl_14, tbl_15, tbl_16, tbl_17, tbl_18, tbl_19, tbl_20, tbl_21, tbl_22, tbl_23, tbl_24, tbl_25, W_top1, b_top1, W_top2, b_top2, W_top3)
    r_bottom_output, ids, tbl_0, tbl_1, tbl_2, tbl_3, tbl_4, tbl_5, tbl_6, tbl_7, tbl_8, tbl_9, tbl_10, tbl_11, tbl_12, tbl_13, tbl_14, tbl_15, tbl_16, tbl_17, tbl_18, tbl_19, tbl_20, tbl_21, tbl_22, tbl_23, tbl_24, tbl_25, W_top1, b_top1, W_top2, b_top2, W_top3 = _rec_inputs()

    def _L0_rec_setup():
        import jax, jax.numpy as jnp
        import numpy as np
        NUM_FEATURES = 27
        _TRIU_I, _TRIU_J = np.triu_indices(NUM_FEATURES, k=1)
        key = jax.random.key(seed)
        k1, k2 = jax.random.split(key)
        bottom_output = jax.random.normal(k1, (2048, 128), dtype=jnp.float32)
        embeddings = jax.random.normal(k2, (2048, 26, 128), dtype=jnp.float32)
        return {'bottom_output': bottom_output, 'embeddings': embeddings}
    _L0_rec_all = _L0_rec_setup()
    _L0_rec_in = {k: v for k, v in _L0_rec_all.items() if k in ()}
    del _L0_rec_all
    return {'r_bottom_output': r_bottom_output, 'ids': ids, 'tbl_0': tbl_0, 'tbl_1': tbl_1, 'tbl_2': tbl_2, 'tbl_3': tbl_3, 'tbl_4': tbl_4, 'tbl_5': tbl_5, 'tbl_6': tbl_6, 'tbl_7': tbl_7, 'tbl_8': tbl_8, 'tbl_9': tbl_9, 'tbl_10': tbl_10, 'tbl_11': tbl_11, 'tbl_12': tbl_12, 'tbl_13': tbl_13, 'tbl_14': tbl_14, 'tbl_15': tbl_15, 'tbl_16': tbl_16, 'tbl_17': tbl_17, 'tbl_18': tbl_18, 'tbl_19': tbl_19, 'tbl_20': tbl_20, 'tbl_21': tbl_21, 'tbl_22': tbl_22, 'tbl_23': tbl_23, 'tbl_24': tbl_24, 'tbl_25': tbl_25, 'W_top1': W_top1, 'b_top1': b_top1, 'W_top2': W_top2, 'b_top2': b_top2, 'W_top3': W_top3}

def reference(r_bottom_output, ids, tbl_0, tbl_1, tbl_2, tbl_3, tbl_4, tbl_5, tbl_6, tbl_7, tbl_8, tbl_9, tbl_10, tbl_11, tbl_12, tbl_13, tbl_14, tbl_15, tbl_16, tbl_17, tbl_18, tbl_19, tbl_20, tbl_21, tbl_22, tbl_23, tbl_24, tbl_25, W_top1, b_top1, W_top2, b_top2, W_top3):
    import jax
    import jax.numpy as jnp

    def _L0_rec_ref(bottom_output, embeddings):
        import jax, jax.numpy as jnp
        import numpy as np
        NUM_FEATURES = 27
        _TRIU_I, _TRIU_J = np.triu_indices(NUM_FEATURES, k=1)
        all_emb = jnp.concatenate([bottom_output[:, None, :], embeddings], axis=1)
        gram = jnp.einsum('bfd,bgd->bfg', all_emb, all_emb)
        return gram[:, _TRIU_I, _TRIU_J]
    e = jnp.stack([tbl_0[ids[:, 0]], tbl_1[ids[:, 1]], tbl_2[ids[:, 2]], tbl_3[ids[:, 3]], tbl_4[ids[:, 4]], tbl_5[ids[:, 5]], tbl_6[ids[:, 6]], tbl_7[ids[:, 7]], tbl_8[ids[:, 8]], tbl_9[ids[:, 9]], tbl_10[ids[:, 10]], tbl_11[ids[:, 11]], tbl_12[ids[:, 12]], tbl_13[ids[:, 13]], tbl_14[ids[:, 14]], tbl_15[ids[:, 15]], tbl_16[ids[:, 16]], tbl_17[ids[:, 17]], tbl_18[ids[:, 18]], tbl_19[ids[:, 19]], tbl_20[ids[:, 20]], tbl_21[ids[:, 21]], tbl_22[ids[:, 22]], tbl_23[ids[:, 23]], tbl_24[ids[:, 24]], tbl_25[ids[:, 25]]], axis=1)
    z = _L0_rec_ref(r_bottom_output, e)
    z = z.reshape(z.shape[0], -1)
    h = jnp.concatenate([z, r_bottom_output], axis=1)
    h = jnp.maximum(h @ W_top1 + b_top1, 0.0)
    h = jnp.maximum(h @ W_top2 + b_top2, 0.0)
    y = h @ W_top3
    return y

_drawn_inputs = setup_inputs


def setup_inputs(seed=0):
    import zlib

    import numpy as np

    out = dict(_drawn_inputs(seed))
    spreads = {'b_top1': (0.0, 0.1), 'b_top2': (0.0, 0.1)}
    factors = {}
    for name, (base, spread) in spreads.items():
        noise = np.random.default_rng([zlib.crc32(name.encode()), seed]).standard_normal(out[name].shape)
        drawn = base * np.exp(spread * noise) if base else spread * noise
        out[name] = jnp.asarray(drawn.astype(out[name].dtype))
    for name, factor in factors.items():
        out[name] = (out[name] * factor).astype(out[name].dtype)
    return out
```

```python
import concourse.bass as bass
from concourse import mybir
from contextlib import ExitStack

BATCH, DIM, TABLES = 512, 128, 26
FEATURES = TABLES + 1
SLOTS = 32
TILE = 128
TILES = BATCH // TILE
HID1, HID2 = 512, 256
TURN = 4
COLS = FEATURES - 1
STRIPS = 4
CHUNKS = -(-COLS // STRIPS)
SPG = 4
BGROUPS = 8
BATCHES = TILE // SPG // BGROUPS
TURNS = [list(range(1 + i, min(1 + i + TURN, FEATURES))) for i in range(0, TABLES, TURN)]
NT = len(TURNS)
EVEN, ODD = (NT + 1) // 2, NT // 2
LAST_ROWS = 96


def strip_columns(j, chunks=CHUNKS):
    return sum(1 for q in range(chunks) if 1 + STRIPS * q + j <= COLS)


def dlrm_tower(nc, bottom, ids, tables, w1, w2, b2, w3, out):
    f32, i32 = mybir.dt.float32, mybir.dt.int32
    ALU, ACT = mybir.AluOpType, mybir.ActivationFunctionType

    with ExitStack() as ctx:
        def sb(name, shape, dt=f32):
            return ctx.enter_context(nc.sbuf_tensor(name, shape, dt))

        def ps(name, shape):
            return ctx.enter_context(nc.psum_tensor(name, shape, f32))

        def sem(name):
            return ctx.enter_context(nc.semaphore(name))

        ids_all = sb("ids_all", [128, TILES, TABLES], i32)
        bottom_rows = sb("bottom_rows", [128, TILES, DIM])
        bottom_t = sb("bottom_t", [128, BATCH])
        rows = sb("rows", [128, TABLES, DIM])
        features = sb("features", [128, TILE, SLOTS])
        pairs = sb("pairs", [128, CHUNKS, TILE])
        ident = sb("ident", [128, 128])
        w1_sb = sb("w1_sb", [128, CHUNKS + 1, HID1])
        w2_sb = sb("w2_sb", [128, HID1 // 128, HID2])
        b2_sb = sb("b2_sb", [128, HID2 // 128])
        w3_sb = sb("w3_sb", [128, HID2 // 128])
        h1 = sb("h1", [128, HID1 // 128, TILE])
        h2 = sb("h2", [128, HID2 // 128, TILE])
        y_sb = sb("y_sb", [1, BATCH])

        turn_ps = [ps(f"turn_ps{i}", [128, TURN, TILE]) for i in range(2)]
        prod_ps = [ps(f"prod_ps{i}", [128, BGROUPS, 128]) for i in range(2)]
        h1_ps = ps("h1_ps", [128, HID1 // 128, TILE])
        h2_ps = ps("h2_ps", [128, 4, TILE])

        ids_in = sem("ids_in")
        bottom_in = sem("bottom_in")
        w1_in = sem("w1_in")
        mlp_in = sem("mlp_in")
        rows_in = [sem(f"rows_in{g}") for g in range(NT)]
        ident_zero = sem("ident_zero")
        ident_ready = sem("ident_ready")
        pads_ready = sem("pads_ready")
        bottom_turned = sem("bottom_turned")
        bottom_ready = sem("bottom_ready")
        turned = sem("turned")
        feat_dve = sem("feat_dve")
        feat_act = sem("feat_act")
        bottom_put = sem("bottom_put")
        prods_done = sem("prods_done")
        pairs_dve = sem("pairs_dve")
        pairs_act = sem("pairs_act")
        h1_done = sem("h1_done")
        h1_ready = sem("h1_ready")
        h2_done = sem("h2_done")
        h2_ready = sem("h2_ready")
        y_done = sem("y_done")
        y_ready = sem("y_ready")
        out_done = sem("out_done")

        block = ctx.enter_context(nc.Block())

        @block.sync
        def _(sp):
            sp.dma_start(ids_all[:], ids).then_inc(ids_in, 16)
            sp.dma_start(bottom_rows[:], bottom.rearrange("(t p) d -> p t d", p=TILE)).then_inc(bottom_in, 16)
            sp.dma_start(w1_sb[:], w1.rearrange("(c p) n -> p c n", p=128)).then_inc(w1_in, 16)
            sp.dma_start(w2_sb[:], w2.rearrange("(c p) n -> p c n", p=128)).then_inc(mlp_in, 16)
            sp.dma_start(b2_sb[:], b2).then_inc(mlp_in, 16)
            sp.dma_start(w3_sb[:], w3).then_inc(mlp_in, 16)
            sp.wait_ge(y_ready, TILES)
            sp.dma_start(out.rearrange("b n -> n b"), y_sb[:]).then_inc(out_done, 16)
            sp.wait_ge(out_done, 16)

        @block.gpsimd
        def _(pool):
            nc.gpsimd.memset(ident[:], 0.0).then_inc(ident_zero, 1)
            pool.wait_ge(ident_zero, 1)
            nc.gpsimd.affine_select(out=ident[:], in_=ident[:], compare_op=ALU.not_equal, fill=1.0, base=0,
                                    pattern=[[-1, 128]], channel_multiplier=1).then_inc(ident_ready, 1)
            pool.wait_ge(ids_in, 16)
            for t in range(TILES):
                for g, turn in enumerate(TURNS):
                    if t >= 1:
                        pool.wait_ge(turned, NT * (t - 1) + g + 1)
                    for f in turn:
                        nc.gpsimd.indirect_dma_start(
                            out=rows[:, f - 1, :], out_offset=None, in_=tables[f - 1],
                            in_offset=bass.IndirectOffsetOnAxis(ap=ids_all[:, t, f - 1:f], axis=0),
                        ).then_inc(rows_in[g], 16)

        def copy_features(engine_copy, g):
            turn = TURNS[g]
            dst = features[:, :, turn[0]:turn[-1] + 1].rearrange("p b f -> p f b")
            return engine_copy(dst, turn_ps[g % 2][:, 0:len(turn), :])

        def copy_pairs(engine_copy, k, strips):
            view = pairs[:].rearrange("p q (k m s) -> p k s m q", k=BATCHES, s=SPG)
            for s in strips:
                for j in range(STRIPS):
                    n = strip_columns(j)
                    c = s * COLS + j
                    src = prod_ps[k % 2][32 * s:32 * s + 32, :, c:c + STRIPS * (n - 1) + 1:STRIPS]
                    last = engine_copy(view[32 * j:32 * j + 32, k, s, :, 0:n], src)
            return last

        @block.vector
        def _(dve):
            nc.vector.memset(features[:, :, FEATURES:SLOTS], 0.0)
            nc.vector.memset(pairs[64:96, CHUNKS - 1, :], 1.0).then_inc(pads_ready, 1)
            dve.wait_ge(bottom_turned, 1)
            nc.vector.tensor_copy(bottom_t[:], turn_ps[0][:].rearrange("p t b -> p (t b)")).then_inc(bottom_ready, 1)
            dve.wait_ge(bottom_ready, 1)

            def tile(t):
                for g in range(0, NT, 2):
                    dve.wait_ge(turned, NT * t + g + 1)
                    copy_features(nc.vector.tensor_copy, g).then_inc(feat_dve, 1)
                    if g == 0:
                        nc.vector.tensor_copy(features[:, :, 0],
                                              bottom_t[:, bass.ts(t, TILE)]).then_inc(bottom_put, 1)
                for k in range(BATCHES):
                    dve.wait_ge(prods_done, BATCHES * t + k + 1)
                    copy_pairs(nc.vector.tensor_copy, k, (0, 1)).then_inc(pairs_dve, 1)

            tile(0)
            with dve.Fori(1, TILES) as t:
                tile(t)

        @block.scalar
        def _(act):
            def features_out(t, g):
                act.wait_ge(turned, NT * t + g + 1)
                copy_features(nc.scalar.copy, g).then_inc(feat_act, 1)

            def pairs_out(t):
                for k in range(BATCHES):
                    act.wait_ge(prods_done, BATCHES * t + k + 1)
                    copy_pairs(nc.scalar.copy, k, (2, 3)).then_inc(pairs_act, 1)

            def h1_out(t):
                act.wait_ge(h1_done, t + 1)
                nc.scalar.activation(h1[:], h1_ps[:], ACT.Relu).then_inc(h1_ready, 1)

            def h2_out(t):
                act.wait_ge(h2_done, t + 1)
                for m in range(HID2 // 128):
                    last = nc.scalar.activation(h2[:, m, :], h2_ps[:, m, :], ACT.Relu, bias=b2_sb[:, m:m + 1])
                last.then_inc(h2_ready, 1)

            def y_out(t):
                act.wait_ge(y_done, t + 1)
                nc.scalar.copy(y_sb[0:1, bass.ts(t, TILE)], h2_ps[0:1, 2, :]).then_inc(y_ready, 1)

            act.wait_ge(mlp_in, 48)
            for g in range(1, NT, 2):
                features_out(0, g)
            pairs_out(0)
            with act.Fori(1, TILES) as t:
                h1_out(t - 1)
                features_out(t, 1)
                h2_out(t - 1)
                y_out(t - 1)
                for g in range(3, NT, 2):
                    features_out(t, g)
                pairs_out(t)
            h1_out(TILES - 1)
            h2_out(TILES - 1)
            y_out(TILES - 1)

        @block.tensor
        def _(pe):
            def turn(t, g):
                pe.wait_ge(rows_in[g], 16 * len(TURNS[g]) * (t + 1))
                if g >= 2:
                    if g % 2 == 0:
                        pe.wait_ge(feat_dve, EVEN * t + g // 2)
                    else:
                        pe.wait_ge(feat_act, ODD * t + g // 2)
                for i, f in enumerate(TURNS[g]):
                    last = nc.tensor.transpose(turn_ps[g % 2][:, i, :], rows[:, f - 1, :], ident[:])
                last.then_inc(turned, 1)

            def products(t, first):
                pe.wait_ge(feat_dve, EVEN * (t + 1))
                pe.wait_ge(feat_act, ODD * (t + 1))
                pe.wait_ge(bottom_put, t + 1)
                for k in range(BATCHES):
                    if not (first and k < 2):
                        pe.wait_ge(pairs_dve, BATCHES * t + k - 1)
                        pe.wait_ge(pairs_act, BATCHES * t + k - 1)
                    for m in range(BGROUPS):
                        b = (k * BGROUPS + m) * SPG
                        last = nc.tensor.matmul(
                            prod_ps[k % 2][:, m, 0:SPG * COLS],
                            features[:, b:b + SPG, :].rearrange("p b f -> p (b f)"),
                            features[:, b:b + SPG, 1:FEATURES], start=True, stop=True)
                    last.then_inc(prods_done, 1)

            def layer1(t):
                pe.wait_ge(pairs_dve, BATCHES * (t + 1))
                pe.wait_ge(pairs_act, BATCHES * (t + 1))
                for n in range(HID1 // 128):
                    for c in range(CHUNKS + 1):
                        k = LAST_ROWS if c == CHUNKS - 1 else 128
                        rhs = bottom_t[:, bass.ts(t, TILE)] if c == CHUNKS else pairs[0:k, c, :]
                        last = nc.tensor.matmul(h1_ps[:, n, :], w1_sb[0:k, c, 128 * n:128 * n + 128], rhs,
                                                start=(c == 0), stop=(c == CHUNKS))
                last.then_inc(h1_done, 1)

            def layer2(t, first):
                pe.wait_ge(h1_ready, t + 1)
                if not first:
                    pe.wait_ge(y_ready, t)
                for m in range(HID2 // 128):
                    for c in range(HID1 // 128):
                        last = nc.tensor.matmul(h2_ps[:, m, :], w2_sb[:, c, 128 * m:128 * m + 128], h1[:, c, :],
                                                start=(c == 0), stop=(c == HID1 // 128 - 1))
                last.then_inc(h2_done, 1)

            def layer3(t):
                pe.wait_ge(h2_ready, t + 1)
                for m in range(HID2 // 128):
                    last = nc.tensor.matmul(h2_ps[0:1, 2, :], w3_sb[:, m:m + 1], h2[:, m, :],
                                            start=(m == 0), stop=(m == HID2 // 128 - 1))
                last.then_inc(y_done, 1)

            pe.wait_ge(ident_ready, 1)
            pe.wait_ge(bottom_in, 16)
            for t in range(TILES):
                last = nc.tensor.transpose(turn_ps[0][:, t, :], bottom_rows[:, t, :], ident[:])
            last.then_inc(bottom_turned, 1)
            pe.wait_ge(bottom_ready, 1)
            pe.wait_ge(pads_ready, 1)
            for g in range(NT):
                turn(0, g)
            products(0, True)
            pe.wait_ge(w1_in, 16)
            pe.wait_ge(mlp_in, 48)

            turn_ahead = 1
            def overlapped(t, first):
                turn(t, 0)
                layer1(t - 1)
                turn(t, 1)
                layer2(t - 1, first)
                turn(t, 2)
                layer3(t - 1)
                for g in range(3, NT):
                    turn(t, g)
                products(t, False)

            overlapped(1, True)
            with pe.Fori(2, TILES) as t:
                overlapped(t, False)
            layer1(TILES - 1)
            layer2(TILES - 1, False)
            layer3(TILES - 1)


_TABLES = [f"tbl_{f}" for f in range(TABLES)]


def kernel(**inputs):
    import numpy as _np
    import concourse.bacc as _bacc
    from concourse import mybir as _mybir
    from concourse.bass_utils import run_bass_kernel_spmd as _run

    arrays = {n: _np.ascontiguousarray(inputs[n]) for n in ["r_bottom_output", "W_top2"] + _TABLES}
    for n in ("b_top2", "W_top3"):
        arrays[n] = _np.ascontiguousarray(_np.asarray(inputs[n]).reshape(HID2 // 128, 128).T)
    ids = _np.asarray(inputs["ids"])
    arrays["ids"] = _np.ascontiguousarray(ids.reshape(TILES, TILE, TABLES).transpose(1, 0, 2))
    w = _np.asarray(inputs["W_top1"])
    w1 = _np.zeros(((CHUNKS + 1) * 128, HID1), w.dtype)
    first, second = _np.triu_indices(FEATURES, k=1)
    w1[128 * ((second - 1) // STRIPS) + 32 * ((second - 1) % STRIPS) + first] = w[:len(first)]
    w1[128 * (CHUNKS - 1) + 64] = _np.asarray(inputs["b_top1"])
    w1[128 * CHUNKS:] = w[len(first):]
    arrays["W_top1"] = w1

    nc = _bacc.Bacc("TRN2", target_bir_lowering=False, num_devices=1)
    ap = {n: nc.dram_tensor(f"in_{n}_dram", a.shape, _mybir.dt.from_np(a.dtype), kind="ExternalInput").ap()
          for n, a in arrays.items()}
    out = nc.dram_tensor("out_0_dram", (BATCH, 1), _mybir.dt.float32, kind="ExternalOutput").ap()
    dlrm_tower(nc, ap["r_bottom_output"], ap["ids"], [ap[n] for n in _TABLES], ap["W_top1"], ap["W_top2"],
               ap["b_top2"], ap["W_top3"], out)
    r = _run(nc, [{f"in_{n}_dram": a for n, a in arrays.items()}], core_ids=[0])
    return r.results[0]["out_0_dram"]
```

```python
import concourse.bass as bass
from concourse import mybir
from contextlib import ExitStack

BATCH, DIM, TABLES = 512, 128, 26
FEATURES = TABLES + 1
SLOTS = 32
TILE = 128
TILES = BATCH // TILE
HID1, HID2 = 512, 256
TURN = 4
COLS = FEATURES - 1
STRIPS = 4
CHUNKS = -(-COLS // STRIPS)
SPG = 4
BGROUPS = 8
BATCHES = TILE // SPG // BGROUPS
PICKED = [1, 2, 4, 5, 11]
PICKS = len(PICKED)
GATHERED = [f for f in range(TABLES) if f not in PICKED]
ORDER = PICKED + GATHERED
PICK_ROWS = 1000
RPP = -(-PICK_ROWS // 128)
FIRST_G = 1 + PICKS
TURNS = [list(range(i, min(i + TURN, FEATURES))) for i in range(FIRST_G, FEATURES, TURN)]
NT = len(TURNS)
EVEN, ODD = (NT + 1) // 2, NT // 2
LAST_ROWS = 96


OPENING_PE, OPENING_DVE, OPENING_ACT = [], [], []
for _i in range(max(PICKS, NT + 2)):
    if _i < PICKS:
        OPENING_PE.append(("pick", _i))
        OPENING_DVE.append(("pick", _i))
        OPENING_ACT.append(("high", _i))
    if _i == 0:
        OPENING_DVE.append(("bottom", 0))
    if 1 <= _i <= NT:
        OPENING_PE.append(("turn", _i - 1))
    if 1 <= _i <= PICKS:
        OPENING_ACT.append(("out", _i - 1))
    if 2 <= _i <= NT + 1:
        (OPENING_ACT if _i % 2 else OPENING_DVE).append(("turn", _i - 2))
if PICKS == max(PICKS, NT + 2):
    OPENING_ACT.append(("out", PICKS - 1))


def strip_columns(j):
    return sum(1 for q in range(CHUNKS) if 1 + STRIPS * q + j <= COLS)


def dlrm_tower(nc, bottom, ids, picked_ids, picked, tables, w1, w2, b2, w3, out):
    f32, f32r, i32 = mybir.dt.float32, mybir.dt.float32r, mybir.dt.int32
    ALU, ACT = mybir.AluOpType, mybir.ActivationFunctionType

    with ExitStack() as ctx:
        def sb(name, shape, dt=f32):
            return ctx.enter_context(nc.sbuf_tensor(name, shape, dt))

        def ps(name, shape):
            return ctx.enter_context(nc.psum_tensor(name, shape, f32))

        def sem(name):
            return ctx.enter_context(nc.semaphore(name))

        ids_all = sb("ids_all", [128, TILES, TABLES], i32)
        ids_wide = sb("ids_wide", [128, PICKS, BATCH], i32)
        row_int = sb("row_int", [128, RPP], i32)
        row_of = sb("row_of", [128, RPP])
        table_raw = [sb(f"table_raw{i}", [128, RPP, DIM]) for i in range(2)]
        table_hi = [sb(f"table_hi{i}", [128, RPP, DIM], f32r) for i in range(2)]
        table_lo = [sb(f"table_lo{i}", [128, RPP, DIM], f32r) for i in range(2)]
        onehot = [sb(f"onehot{i}", [128, RPP, BATCH], f32r) for i in range(2)]
        picks = sb("picks", [128, PICKS, BATCH])
        bottom_rows = sb("bottom_rows", [128, TILES, DIM])
        bottom_t = sb("bottom_t", [128, BATCH])
        rows = sb("rows", [128, FEATURES - FIRST_G, DIM])
        features = sb("features", [128, TILE, SLOTS])
        pairs = sb("pairs", [128, CHUNKS, TILE])
        ident = sb("ident", [128, 128])
        w1_sb = sb("w1_sb", [128, CHUNKS + 1, HID1])
        w2_sb = sb("w2_sb", [128, HID1 // 128, HID2])
        b2_sb = sb("b2_sb", [128, HID2 // 128])
        w3_sb = sb("w3_sb", [128, HID2 // 128])
        h1 = sb("h1", [128, HID1 // 128, TILE])
        h2 = sb("h2", [128, HID2 // 128, TILE])
        y_sb = sb("y_sb", [1, BATCH])

        turn_ps = [ps(f"turn_ps{i}", [128, TURN, TILE]) for i in range(2)]
        prod_ps = [ps(f"prod_ps{i}", [128, BGROUPS, 128]) for i in range(2)]
        h1_ps = ps("h1_ps", [128, HID1 // 128, TILE])
        h2_ps = ps("h2_ps", [128, 4, TILE])
        pick_ps = [h1_ps, h2_ps]
        ids_in = sem("ids_in")
        wide_in = [sem(f"wide_in{i}") for i in range(PICKS)]
        table_in = [sem(f"table_in{i}") for i in range(2)]
        bottom_in = sem("bottom_in")
        w1_in = sem("w1_in")
        mlp_in = sem("mlp_in")
        rows_in = [sem(f"rows_in{g}") for g in range(NT)]
        ident_zero = sem("ident_zero")
        ident_ready = sem("ident_ready")
        row_int_ready = sem("row_int_ready")
        row_of_ready = sem("row_of_ready")
        hi_ready = sem("hi_ready")
        lo_ready = sem("lo_ready")
        onehot_ready = sem("onehot_ready")
        picked_done = sem("picked_done")
        picks_ready = sem("picks_ready")
        pads_ready = sem("pads_ready")
        bottom_turned = sem("bottom_turned")
        bottom_ready = sem("bottom_ready")
        turned = sem("turned")
        feat_dve = sem("feat_dve")
        feat_act = sem("feat_act")
        static_put = sem("static_put")
        prods_done = sem("prods_done")
        pairs_dve = sem("pairs_dve")
        pairs_act = sem("pairs_act")
        h1_done = sem("h1_done")
        h1_ready = sem("h1_ready")
        h2_done = sem("h2_done")
        h2_ready = sem("h2_ready")
        y_done = sem("y_done")
        y_ready = sem("y_ready")
        out_done = sem("out_done")

        block = ctx.enter_context(nc.Block())

        @block.sync
        def _(sp):
            sp.dma_start(ids_all[:], ids).then_inc(ids_in, 16)
            for i in range(PICKS):
                sp.dma_start(ids_wide[:, i, :], picked_ids[i].partition_broadcast(128)).then_inc(wide_in[i], 16)
                if i >= 2:
                    sp.wait_ge(lo_ready, i - 1)
                    sp.wait_ge(hi_ready, i - 1)
                sp.dma_start(table_raw[i % 2][:], picked[i]).then_inc(table_in[i % 2], 16)
                if i == 0:
                    sp.dma_start(bottom_rows[:], bottom.rearrange("(t p) d -> p t d", p=TILE)).then_inc(bottom_in, 16)
            for c in range(CHUNKS + 1):
                sp.dma_start(w1_sb[:, c, :], w1[128 * c:128 * c + 128, :]).then_inc(w1_in, 16)
            sp.dma_start(w2_sb[:], w2.rearrange("(c p) n -> p c n", p=128)).then_inc(mlp_in, 16)
            sp.dma_start(b2_sb[:], b2).then_inc(mlp_in, 16)
            sp.dma_start(w3_sb[:], w3).then_inc(mlp_in, 16)
            sp.wait_ge(y_ready, TILES)
            sp.dma_start(out.rearrange("b n -> n b"), y_sb[:]).then_inc(out_done, 16)
            sp.wait_ge(out_done, 16)

        @block.gpsimd
        def _(pool):
            nc.gpsimd.iota(row_int[:], pattern=[[1, RPP]], base=0, channel_multiplier=RPP).then_inc(row_int_ready, 1)
            nc.gpsimd.memset(ident[:], 0.0).then_inc(ident_zero, 1)
            pool.wait_ge(ident_zero, 1)
            nc.gpsimd.affine_select(out=ident[:], in_=ident[:], compare_op=ALU.not_equal, fill=1.0, base=0,
                                    pattern=[[-1, 128]], channel_multiplier=1).then_inc(ident_ready, 1)
            pool.wait_ge(ids_in, 16)
            for t in range(TILES):
                for g, turn in enumerate(TURNS):
                    if t >= 1:
                        pool.wait_ge(turned, NT * (t - 1) + g + 1)
                    for slot in turn:
                        table = ORDER[slot - 1]
                        nc.gpsimd.indirect_dma_start(
                            out=rows[:, slot - FIRST_G, :], out_offset=None, in_=tables[table],
                            in_offset=bass.IndirectOffsetOnAxis(ap=ids_all[:, t, table:table + 1], axis=0),
                        ).then_inc(rows_in[g], 16)

        def copy_features(engine_copy, g):
            turn = TURNS[g]
            dst = features[:, :, turn[0]:turn[-1] + 1].rearrange("p b f -> p f b")
            return engine_copy(dst, turn_ps[g % 2][:, 0:len(turn), :])

        def copy_pairs(engine_copy, k, strips):
            view = pairs[:].rearrange("p q (k m s) -> p k s m q", k=BATCHES, s=SPG)
            for s in strips:
                for j in range(STRIPS):
                    n = strip_columns(j)
                    c = s * COLS + j
                    src = prod_ps[k % 2][32 * s:32 * s + 32, :, c:c + STRIPS * (n - 1) + 1:STRIPS]
                    last = engine_copy(view[32 * j:32 * j + 32, k, s, :, 0:n], src)
            return last

        @block.vector
        def _(dve):
            def pick_operands(i):
                dve.wait_ge(wide_in[i], 16)
                if i >= 2:
                    dve.wait_ge(picked_done, i - 1)
                for c in range(RPP):
                    nc.vector.tensor_scalar(onehot[i % 2][:, c, :], ids_wide[:, i, :], row_of[:, c:c + 1],
                                            None, ALU.is_equal).then_inc(onehot_ready, 1)
                dve.wait_ge(table_in[i % 2], 16 * (i // 2 + 1))
                dve.wait_ge(hi_ready, i + 1)
                nc.vector.tensor_tensor(table_lo[i % 2][:], table_raw[i % 2][:], table_hi[i % 2][:].bitcast(f32),
                                        ALU.subtract).then_inc(lo_ready, 1)

            def features_out(t, g):
                dve.wait_ge(turned, NT * t + g + 1)
                copy_features(nc.vector.tensor_copy, g).then_inc(feat_dve, 1)

            def static_features(t):
                nc.vector.tensor_copy(features[:, :, 0], bottom_t[:, bass.ts(t, TILE)])
                nc.vector.tensor_copy(features[:, :, 1:FIRST_G].rearrange("p b f -> p f b"),
                                      picks[:, :, bass.ts(t, TILE)]).then_inc(static_put, 1)

            def pairs_out(t):
                for k in range(BATCHES):
                    dve.wait_ge(prods_done, BATCHES * t + k + 1)
                    copy_pairs(nc.vector.tensor_copy, k, (0, 1)).then_inc(pairs_dve, 1)

            nc.vector.memset(features[:, :, FEATURES:SLOTS], 0.0)
            nc.vector.memset(pairs[64:96, CHUNKS - 1, :], 1.0).then_inc(pads_ready, 1)
            dve.wait_ge(row_int_ready, 1)
            nc.vector.tensor_copy(row_of[:], row_int[:]).then_inc(row_of_ready, 1)
            dve.wait_ge(row_of_ready, 1)
            for kind, n in OPENING_DVE:
                if kind == "pick":
                    pick_operands(n)
                elif kind == "turn":
                    features_out(0, n)
                else:
                    dve.wait_ge(bottom_turned, 1)
                    nc.vector.tensor_copy(bottom_t[:], turn_ps[1][:].rearrange("p t b -> p (t b)")
                                          ).then_inc(bottom_ready, 1)
            dve.wait_ge(bottom_ready, 1)
            dve.wait_ge(picks_ready, PICKS)
            static_features(0)
            pairs_out(0)
            with dve.Fori(1, TILES) as t:
                static_features(t)
                for g in range(0, NT, 2):
                    features_out(t, g)
                pairs_out(t)

        @block.scalar
        def _(act):
            def table_high(i):
                act.wait_ge(table_in[i % 2], 16 * (i // 2 + 1))
                if i >= 2:
                    act.wait_ge(picked_done, i - 1)
                nc.scalar.copy(table_hi[i % 2][:], table_raw[i % 2][:]).then_inc(hi_ready, 1)

            def pick_out(i):
                act.wait_ge(picked_done, i + 1)
                nc.scalar.copy(picks[:, i, :], pick_ps[i % 2][:].rearrange("p a b -> p (a b)")
                               ).then_inc(picks_ready, 1)

            def features_out(t, g):
                act.wait_ge(turned, NT * t + g + 1)
                copy_features(nc.scalar.copy, g).then_inc(feat_act, 1)

            def pairs_out(t):
                for k in range(BATCHES):
                    act.wait_ge(prods_done, BATCHES * t + k + 1)
                    copy_pairs(nc.scalar.copy, k, (2, 3)).then_inc(pairs_act, 1)

            def h1_out(t):
                act.wait_ge(h1_done, t + 1)
                nc.scalar.activation(h1[:], h1_ps[:], ACT.Relu).then_inc(h1_ready, 1)

            def h2_out(t):
                act.wait_ge(h2_done, t + 1)
                for m in range(HID2 // 128):
                    last = nc.scalar.activation(h2[:, m, :], h2_ps[:, m, :], ACT.Relu, bias=b2_sb[:, m:m + 1])
                last.then_inc(h2_ready, 1)

            def y_out(t):
                act.wait_ge(y_done, t + 1)
                nc.scalar.copy(y_sb[0:1, bass.ts(t, TILE)], h2_ps[0:1, 2, :]).then_inc(y_ready, 1)

            for kind, n in OPENING_ACT:
                if kind == "high":
                    table_high(n)
                elif kind == "out":
                    pick_out(n)
                else:
                    features_out(0, n)
            pairs_out(0)
            act.wait_ge(mlp_in, 48)
            with act.Fori(1, TILES) as t:
                features_out(t, 1)
                h1_out(t - 1)
                features_out(t, 3)
                h2_out(t - 1)
                if NT > 5:
                    features_out(t, 5)
                y_out(t - 1)
                pairs_out(t)
            h1_out(TILES - 1)
            h2_out(TILES - 1)
            y_out(TILES - 1)

        @block.tensor
        def _(pe):
            def pick(i):
                pe.wait_ge(hi_ready, i + 1)
                if i >= 2:
                    pe.wait_ge(picks_ready, i - 1)
                acc = pick_ps[i % 2][:].rearrange("p a b -> p (a b)")
                for c in range(RPP):
                    pe.wait_ge(onehot_ready, RPP * i + c + 1)
                    nc.tensor.matmul(acc, table_hi[i % 2][:, c, :], onehot[i % 2][:, c, :], start=(c == 0), stop=False)
                pe.wait_ge(lo_ready, i + 1)
                for c in range(RPP):
                    last = nc.tensor.matmul(acc, table_lo[i % 2][:, c, :], onehot[i % 2][:, c, :],
                                            start=False, stop=(c == RPP - 1))
                last.then_inc(picked_done, 1)

            def turn(t, g):
                pe.wait_ge(rows_in[g], 16 * len(TURNS[g]) * (t + 1))
                if g >= 2:
                    if g % 2 == 0:
                        pe.wait_ge(feat_dve, EVEN * t + g // 2)
                    else:
                        pe.wait_ge(feat_act, ODD * t + g // 2)
                for i, slot in enumerate(TURNS[g]):
                    last = nc.tensor.transpose(turn_ps[g % 2][:, i, :], rows[:, slot - FIRST_G, :], ident[:])
                last.then_inc(turned, 1)

            def products(t, first):
                pe.wait_ge(static_put, t + 1)
                pe.wait_ge(feat_dve, EVEN * (t + 1))
                pe.wait_ge(feat_act, ODD * (t + 1))
                for k in range(BATCHES):
                    if not (first and k < 2):
                        pe.wait_ge(pairs_dve, BATCHES * t + k - 1)
                        pe.wait_ge(pairs_act, BATCHES * t + k - 1)
                    for m in range(BGROUPS):
                        b = (k * BGROUPS + m) * SPG
                        last = nc.tensor.matmul(
                            prod_ps[k % 2][:, m, 0:SPG * COLS],
                            features[:, b:b + SPG, :].rearrange("p b f -> p (b f)"),
                            features[:, b:b + SPG, 1:FEATURES], start=True, stop=True)
                    last.then_inc(prods_done, 1)

            def layer1(t):
                pe.wait_ge(pairs_dve, BATCHES * (t + 1))
                pe.wait_ge(pairs_act, BATCHES * (t + 1))
                for n in range(HID1 // 128):
                    for c in range(CHUNKS + 1):
                        k = LAST_ROWS if c == CHUNKS - 1 else 128
                        rhs = bottom_t[:, bass.ts(t, TILE)] if c == CHUNKS else pairs[0:k, c, :]
                        last = nc.tensor.matmul(h1_ps[:, n, :], w1_sb[0:k, c, 128 * n:128 * n + 128], rhs,
                                                start=(c == 0), stop=(c == CHUNKS))
                last.then_inc(h1_done, 1)

            def layer2(t):
                pe.wait_ge(h1_ready, t + 1)
                for m in range(HID2 // 128):
                    for c in range(HID1 // 128):
                        last = nc.tensor.matmul(h2_ps[:, m, :], w2_sb[:, c, 128 * m:128 * m + 128], h1[:, c, :],
                                                start=(c == 0), stop=(c == HID1 // 128 - 1))
                last.then_inc(h2_done, 1)

            def layer3(t):
                pe.wait_ge(h2_ready, t + 1)
                for m in range(HID2 // 128):
                    last = nc.tensor.matmul(h2_ps[0:1, 2, :], w3_sb[:, m:m + 1], h2[:, m, :],
                                            start=(m == 0), stop=(m == HID2 // 128 - 1))
                last.then_inc(y_done, 1)

            pe.wait_ge(ident_ready, 1)
            pe.wait_ge(bottom_in, 16)
            for t in range(TILES):
                last = nc.tensor.transpose(turn_ps[1][:, t, :], bottom_rows[:, t, :], ident[:])
            last.then_inc(bottom_turned, 1)
            for kind, n in OPENING_PE:
                if kind == "pick":
                    pick(n)
                else:
                    if n == 1:
                        pe.wait_ge(bottom_ready, 1)
                    turn(0, n)
            pe.wait_ge(pads_ready, 1)
            products(0, True)
            pe.wait_ge(w1_in, 16 * (CHUNKS + 1))
            pe.wait_ge(mlp_in, 48)
            with pe.Fori(1, TILES) as t:
                turn(t, 0)
                turn(t, 1)
                layer1(t - 1)
                turn(t, 2)
                turn(t, 3)
                layer2(t - 1)
                for g in range(4, NT):
                    turn(t, g)
                layer3(t - 1)
                products(t, False)
                pe.wait_ge(y_ready, t)
            layer1(TILES - 1)
            layer2(TILES - 1)
            layer3(TILES - 1)


_GATHERED = [f"tbl_{f}" for f in GATHERED]


def kernel(**inputs):
    import numpy as _np
    import concourse.bacc as _bacc
    from concourse import mybir as _mybir
    from concourse.bass_utils import run_bass_kernel_spmd as _run

    arrays = {n: _np.ascontiguousarray(inputs[n]) for n in ["r_bottom_output", "W_top2"] + _GATHERED}
    for n in ("b_top2", "W_top3"):
        arrays[n] = _np.ascontiguousarray(_np.asarray(inputs[n]).reshape(HID2 // 128, 128).T)
    ids = _np.asarray(inputs["ids"])
    arrays["picked_ids"] = _np.ascontiguousarray(ids[:, PICKED].T)
    picked = _np.zeros((PICKS, 128 * RPP, DIM), _np.float32)
    for i, f in enumerate(PICKED):
        picked[i, :PICK_ROWS] = _np.asarray(inputs[f"tbl_{f}"])
    arrays["picked"] = picked.reshape(PICKS, 128, RPP, DIM)
    arrays["ids"] = _np.ascontiguousarray(ids.reshape(TILES, TILE, TABLES).transpose(1, 0, 2))
    w = _np.asarray(inputs["W_top1"])
    w1 = _np.zeros(((CHUNKS + 1) * 128, HID1), w.dtype)
    pair_row = _np.zeros((FEATURES, FEATURES), _np.int64)
    first, second = _np.triu_indices(FEATURES, k=1)
    pair_row[first, second] = pair_row[second, first] = _np.arange(len(first))
    feature = _np.array([0] + [1 + f for f in ORDER])
    w1[128 * ((second - 1) // STRIPS) + 32 * ((second - 1) % STRIPS) + first] = \
        w[pair_row[feature[first], feature[second]]]
    w1[128 * (CHUNKS - 1) + 64] = _np.asarray(inputs["b_top1"])
    w1[128 * CHUNKS:] = w[len(first):]
    arrays["W_top1"] = w1

    nc = _bacc.Bacc("TRN2", target_bir_lowering=False, num_devices=1)
    ap = {n: nc.dram_tensor(f"in_{n}_dram", a.shape, _mybir.dt.from_np(a.dtype), kind="ExternalInput").ap()
          for n, a in arrays.items()}
    out = nc.dram_tensor("out_0_dram", (BATCH, 1), _mybir.dt.float32, kind="ExternalOutput").ap()
    dlrm_tower(nc, ap["r_bottom_output"], ap["ids"], ap["picked_ids"], ap["picked"],
               {f: ap[f"tbl_{f}"] for f in GATHERED}, ap["W_top1"], ap["W_top2"],
               ap["b_top2"], ap["W_top3"], out)
    r = _run(nc, [{f"in_{n}_dram": a for n, a in arrays.items()}], core_ids=[0])
    return r.results[0]["out_0_dram"]
```

```python
import concourse.bass as bass
from concourse import mybir
from contextlib import ExitStack

BATCH, DIM, TABLES = 512, 128, 26
FEATURES = TABLES + 1
SLOTS = 32
TILE = 128
TILES = BATCH // TILE
HID1, HID2 = 512, 256
TURN = 4
COLS = FEATURES - 1
STRIPS = 4
CHUNKS = -(-COLS // STRIPS)
SPG = 4
FIRSTS = (SPG - 1) * SLOTS + COLS
BGROUPS = 8
BATCHES = TILE // SPG // BGROUPS
PICKED = [1, 2, 4, 5, 11, 13, 14]
PICKS = len(PICKED)
GATHERED = [f for f in range(TABLES) if f not in PICKED]
ORDER = PICKED + GATHERED
PICK_ROWS = 1000
RPP = -(-PICK_ROWS // 128)
WARM_UP = 10
HALF = RPP // 2
ACT_RPP = 2
FIRST_G = 1 + PICKS
TURNS = [list(range(i, min(i + TURN, FEATURES - 2))) for i in range(FIRST_G, FEATURES - 2, TURN)]
TURNS.append([FEATURES - 2, FEATURES - 1])
NT = len(TURNS)
EVEN, ODD = (NT + 1) // 2, NT // 2
LAST_ROWS = 96

PLACES = list(range(HALF, RPP)) + list(range(ACT_RPP, HALF)) + list(range(ACT_RPP))

OPENING_PE, OPENING_DVE, OPENING_ACT = [], [], []
for _i in range(PICKS):
    OPENING_PE.append(("pick", _i))
    OPENING_DVE.append(("pick", _i))
    OPENING_ACT.append(("high", _i))
    if _i == 0:
        OPENING_PE.append(("bottom", 0))
    if _i == 1:
        OPENING_DVE.append(("bottom", 0))
    if 1 <= _i < PICKS:
        OPENING_ACT.append(("out", _i - 1))
    _last = PICKS - 2
    for _g in range(NT):
        if min(_g + 1, _last) == _i:
            OPENING_PE.append(("turn", _g))
        if min(_g + 1, _last) == _i - 1:
            (OPENING_ACT if _g % 2 else OPENING_DVE).append(("turn", _g))


def strip_columns(j):
    return sum(1 for q in range(CHUNKS) if 1 + STRIPS * q + j <= COLS)


def dlrm_tower(nc, bottom, ids, picked_ids, picked, tables, w1, w2, b2, w3, out):
    f32, f32r, i32 = mybir.dt.float32, mybir.dt.float32r, mybir.dt.int32
    ALU, ACT = mybir.AluOpType, mybir.ActivationFunctionType

    with ExitStack() as ctx:
        def sb(name, shape, dt=f32):
            return ctx.enter_context(nc.sbuf_tensor(name, shape, dt))

        def ps(name, shape):
            return ctx.enter_context(nc.psum_tensor(name, shape, f32))

        def sem(name):
            return ctx.enter_context(nc.semaphore(name))

        ids_all = sb("ids_all", [128, TILES, TABLES], i32)
        ids_wide = sb("ids_wide", [128, PICKS, BATCH], i32)
        row_int = sb("row_int", [128, RPP], i32)
        row_of = sb("row_of", [128, RPP])
        minus_row = sb("minus_row", [128, RPP])
        distance = sb("distance", [128, ACT_RPP, BATCH])
        table_raw = [sb(f"table_raw{i}", [128, RPP, DIM]) for i in range(2)]
        table_hi = [sb(f"table_hi{i}", [128, RPP, DIM], f32r) for i in range(2)]
        table_lo = [sb(f"table_lo{i}", [128, RPP, DIM], f32r) for i in range(2)]
        onehot = [sb(f"onehot{i}", [128, RPP, BATCH], f32r) for i in range(2)]
        static_t = sb("static_t", [128, FIRST_G, BATCH])
        bottom_rows = sb("bottom_rows", [128, TILES, DIM])
        rows = sb("rows", [128, FEATURES - FIRST_G, DIM])
        features = sb("features", [128, TILE, SLOTS])
        pairs = sb("pairs", [128, CHUNKS, TILE])
        ident = sb("ident", [128, 128])
        w1_sb = sb("w1_sb", [128, CHUNKS + 1, HID1])
        w2_sb = sb("w2_sb", [128, HID1 // 128, HID2])
        b2_sb = sb("b2_sb", [128, HID2 // 128])
        w3_sb = sb("w3_sb", [128, HID2 // 128])
        h1 = sb("h1", [128, HID1 // 128, TILE])
        h2 = sb("h2", [128, HID2 // 128, TILE])
        y_sb = sb("y_sb", [1, BATCH])

        turn_ps = [ps(f"turn_ps{i}", [128, TURN, TILE]) for i in range(2)]
        prod_ps = [ps(f"prod_ps{i}", [128, BGROUPS, 128]) for i in range(2)]
        mlp_ps = [ps(f"mlp_ps{i}", [128, 4, TILE]) for i in range(2)]
        pick_ps = mlp_ps

        ids_in = sem("ids_in")
        wide_in = [sem(f"wide_in{i}") for i in range(PICKS)]
        first_half_in = sem("first_half_in")
        first_hi_ready = sem("first_hi_ready")
        first_lo_ready = sem("first_lo_ready")
        table_in = [sem(f"table_in{i}") for i in range(2)]
        bottom_in = sem("bottom_in")
        w1_in = sem("w1_in")
        mlp_in = sem("mlp_in")
        rows_in = [sem(f"rows_in{g}") for g in range(NT)]
        ident_zero = sem("ident_zero")
        ident_ready = sem("ident_ready")
        row_int_ready = sem("row_int_ready")
        row_of_ready = sem("row_of_ready")
        minus_row_ready = sem("minus_row_ready")
        distance_ready = sem("distance_ready")
        onehot_act = sem("onehot_act")
        hi_ready = sem("hi_ready")
        lo_ready = sem("lo_ready")
        onehot_ready = sem("onehot_ready")
        picked_done = sem("picked_done")
        picks_ready = sem("picks_ready")
        pairs_zero = sem("pairs_zero")
        pads_ready = sem("pads_ready")
        last_pick_put = sem("last_pick_put")
        warm_ready = sem("warm_ready")
        bottom_turned = sem("bottom_turned")
        bottom_ready = sem("bottom_ready")
        turned = sem("turned")
        feat_dve = sem("feat_dve")
        feat_act = sem("feat_act")
        static_put = sem("static_put")
        prods_done = sem("prods_done")
        pairs_dve = sem("pairs_dve")
        pairs_act = sem("pairs_act")
        h1_done = sem("h1_done")
        h1_ready = sem("h1_ready")
        h2_done = sem("h2_done")
        h2_ready = sem("h2_ready")
        y_done = sem("y_done")
        y_ready = sem("y_ready")
        out_done = sem("out_done")

        block = ctx.enter_context(nc.Block())

        @block.sync
        def _(sp):
            sp.dma_start(ids_all[:], ids).then_inc(ids_in, 16)
            sp.dma_start(table_raw[0][:, HALF:, :], picked[0][:, HALF:, :]).then_inc(first_half_in, 16)
            sp.dma_start(table_raw[0][:, 0:HALF, :], picked[0][:, 0:HALF, :]).then_inc(table_in[0], 16)
            for i in range(1, PICKS):
                sp.dma_start(ids_wide[:, i, :], picked_ids[i].partition_broadcast(128)).then_inc(wide_in[i], 16)
                if i >= 2:
                    sp.wait_ge(lo_ready, i - 1)
                    sp.wait_ge(hi_ready, i - 1)
                sp.dma_start(table_raw[i % 2][:], picked[i]).then_inc(table_in[i % 2], 16)
                if i == 1:
                    sp.dma_start(bottom_rows[:], bottom.rearrange("(t p) d -> p t d", p=TILE)).then_inc(bottom_in, 16)
            for c in range(CHUNKS + 1):
                sp.dma_start(w1_sb[:, c, :], w1[128 * c:128 * c + 128, :]).then_inc(w1_in, 16)
            sp.dma_start(w2_sb[:], w2.rearrange("(c p) n -> p c n", p=128)).then_inc(mlp_in, 16)
            sp.dma_start(b2_sb[:], b2).then_inc(mlp_in, 16)
            sp.dma_start(w3_sb[:], w3).then_inc(mlp_in, 16)
            sp.wait_ge(y_ready, 1 + TILES)
            sp.dma_start(out.rearrange("b n -> n b"), y_sb[:]).then_inc(out_done, 16)
            sp.wait_ge(out_done, 16)

        @block.gpsimd
        def _(pool):
            nc.gpsimd.iota(row_int[:], pattern=[[1, RPP]], base=0, channel_multiplier=RPP).then_inc(row_int_ready, 1)
            nc.gpsimd.memset(ident[:], 0.0).then_inc(ident_zero, 1)
            pool.wait_ge(ident_zero, 1)
            nc.gpsimd.affine_select(out=ident[:], in_=ident[:], compare_op=ALU.not_equal, fill=1.0, base=0,
                                    pattern=[[-1, 128]], channel_multiplier=1).then_inc(ident_ready, 1)
            nc.gpsimd.memset(features[:, :, FEATURES:SLOTS], 0.0).then_inc(pads_ready, 1)
            nc.gpsimd.memset(pairs[:], 0.0).then_inc(pairs_zero, 1)
            pool.wait_ge(pairs_zero, 1)
            nc.gpsimd.memset(pairs[64:96, CHUNKS - 1, :], 1.0).then_inc(pads_ready, 1)
            pool.wait_ge(ids_in, 16)
            for t in range(TILES):
                for g, turn in enumerate(TURNS):
                    if t >= 1:
                        pool.wait_ge(turned, NT * (t - 1) + g + 1)
                    for slot in turn:
                        table = ORDER[slot - 1]
                        nc.gpsimd.indirect_dma_start(
                            out=rows[:, slot - FIRST_G, :], out_offset=None, in_=tables[table],
                            in_offset=bass.IndirectOffsetOnAxis(ap=ids_all[:, t, table:table + 1], axis=0),
                        ).then_inc(rows_in[g], 16)

        def copy_features(engine_copy, g):
            turn = TURNS[g]
            dst = features[:, :, turn[0]:turn[-1] + 1].rearrange("p b f -> p f b")
            return engine_copy(dst, turn_ps[g % 2][:, 0:len(turn), :])

        def copy_pairs(engine_copy, k, strips):
            view = pairs[:].rearrange("p q (k m s) -> p k s m q", k=BATCHES, s=SPG)
            for s in strips:
                for j in range(STRIPS):
                    n = strip_columns(j)
                    c = s * COLS + j
                    height = min(32, FIRSTS - 32 * s)
                    src = prod_ps[k % 2][32 * s:32 * s + height, :, c:c + STRIPS * (n - 1) + 1:STRIPS]
                    last = engine_copy(view[32 * j:32 * j + height, k, s, :, 0:n], src)
            return last

        @block.vector
        def _(dve):
            def low_half(i, begin, end):
                return nc.vector.tensor_tensor(table_lo[i % 2][:, begin:end, :], table_raw[i % 2][:, begin:end, :],
                                               table_hi[i % 2][:, begin:end, :].bitcast(f32), ALU.subtract)

            def pick_operands(i):
                dve.wait_ge(wide_in[i], 16)
                if i >= 2:
                    dve.wait_ge(picked_done, i - 1)
                for c in PLACES[:-ACT_RPP]:
                    nc.vector.tensor_scalar(onehot[i % 2][:, c, :], ids_wide[:, i, :], row_of[:, c:c + 1],
                                            None, ALU.is_equal).then_inc(onehot_ready, 1)
                if i == 0:
                    dve.wait_ge(first_half_in, 16)
                    dve.wait_ge(first_hi_ready, 1)
                    low_half(0, HALF, RPP).then_inc(first_lo_ready, 1)
                dve.wait_ge(table_in[i % 2], 16 * (i // 2 + 1))
                dve.wait_ge(hi_ready, i + 1)
                low_half(i, 0, HALF if i == 0 else RPP).then_inc(lo_ready, 1)

            def features_out(t, g):
                dve.wait_ge(turned, NT * t + g + 1)
                copy_features(nc.vector.tensor_copy, g).then_inc(feat_dve, 1)

            def static_features(t, first_slot, end_slot):
                return nc.vector.tensor_copy(features[:, :, first_slot:end_slot].rearrange("p b f -> p f b"),
                                             static_t[:, first_slot:end_slot, bass.ts(t, TILE)])

            def pairs_out(t):
                for k in range(BATCHES):
                    dve.wait_ge(prods_done, BATCHES * t + k + 1)
                    copy_pairs(nc.vector.tensor_copy, k, (0, 1)).then_inc(pairs_dve, 1)

            nc.vector.memset(h1[:, 0, :], 0.0).then_inc(warm_ready, 1)
            nc.vector.memset(y_sb[0:1, 0:1], 0.0).then_inc(y_ready, 1)
            dve.wait_ge(row_int_ready, 1)
            nc.vector.tensor_copy(row_of[:], row_int[:]).then_inc(row_of_ready, 1)
            dve.wait_ge(row_of_ready, 1)
            for kind, n in OPENING_DVE:
                if kind == "pick":
                    pick_operands(n)
                elif kind == "turn":
                    features_out(0, n)
                else:
                    dve.wait_ge(bottom_turned, 1)
                    nc.vector.tensor_copy(static_t[:, 0, :], turn_ps[1][:].rearrange("p t b -> p (t b)")
                                          ).then_inc(bottom_ready, 1)
            dve.wait_ge(pads_ready, 2)
            dve.wait_ge(bottom_ready, 1)
            dve.wait_ge(picks_ready, PICKS - 1)
            static_features(0, 0, PICKS).then_inc(static_put, 1)
            pairs_out(0)
            dve.wait_ge(picks_ready, PICKS)
            with dve.Fori(1, TILES) as t:
                static_features(t, 0, FIRST_G).then_inc(static_put, 1)
                for g in range(0, NT, 2):
                    features_out(t, g)
                pairs_out(t)

        @block.scalar
        def _(act):
            def table_high(i):
                act.wait_ge(wide_in[i], 16)
                if i >= 1:
                    act.wait_ge(onehot_act, ACT_RPP * i)
                for c in range(ACT_RPP):
                    nc.scalar.activation(distance[:, c, :], ids_wide[:, i, :], ACT.Abs, bias=minus_row[:, c:c + 1]
                                         ).then_inc(distance_ready, 1)
                    if i == 0 and c == 0:
                        act.wait_ge(first_half_in, 16)
                        nc.scalar.copy(table_hi[0][:, HALF:, :], table_raw[0][:, HALF:, :]
                                       ).then_inc(first_hi_ready, 1)
                act.wait_ge(table_in[i % 2], 16 * (i // 2 + 1))
                if i >= 2:
                    act.wait_ge(picked_done, i - 1)
                end = HALF if i == 0 else RPP
                nc.scalar.copy(table_hi[i % 2][:, 0:end, :], table_raw[i % 2][:, 0:end, :]).then_inc(hi_ready, 1)
                for c in range(ACT_RPP):
                    act.wait_ge(distance_ready, ACT_RPP * i + c + 1)
                    nc.scalar.activation(onehot[i % 2][:, c, :], distance[:, c, :], ACT.Relu, bias=1.0, scale=-4.0
                                         ).then_inc(onehot_act, 1)

            def pick_out(i):
                act.wait_ge(picked_done, i + 1)
                nc.scalar.copy(static_t[:, 1 + i, :], pick_ps[i % 2][:].rearrange("p a b -> p (a b)")
                               ).then_inc(picks_ready, 1)

            def features_out(t, g):
                act.wait_ge(turned, NT * t + g + 1)
                copy_features(nc.scalar.copy, g).then_inc(feat_act, 1)

            def pairs_out(t, first):
                for k in range(BATCHES):
                    act.wait_ge(prods_done, BATCHES * t + k + 1)
                    copy_pairs(nc.scalar.copy, k, (2, 3)).then_inc(pairs_act, 1)
                    if k == 0 and not first:
                        y_out(t - 1)

            def h1_out(t, bank):
                act.wait_ge(h1_done, 2 * t + bank + 1)
                nc.scalar.activation(h1[:, 2 * bank:2 * bank + 2, :], mlp_ps[bank][:, 0:2, :], ACT.Relu
                                     ).then_inc(h1_ready, 1)

            def h2_out(t, bank):
                act.wait_ge(h2_done, 2 * t + bank + 1)
                nc.scalar.activation(h2[:, bank, :], mlp_ps[bank][:, 2, :], ACT.Relu, bias=b2_sb[:, bank:bank + 1]
                                     ).then_inc(h2_ready, 1)

            def y_out(t):
                act.wait_ge(y_done, t + 1)
                nc.scalar.copy(y_sb[0:1, bass.ts(t, TILE)], mlp_ps[0][0:1, 3, :]).then_inc(y_ready, 1)

            act.dma_start(ids_wide[:, 0, :], picked_ids[0].partition_broadcast(128)).then_inc(wide_in[0], 16)
            act.wait_ge(row_int_ready, 1)
            nc.scalar.activation(minus_row[:], row_int[:], ACT.Copy, scale=-1.0).then_inc(minus_row_ready, 1)
            act.wait_ge(minus_row_ready, 1)
            for kind, n in OPENING_ACT:
                if kind == "high":
                    table_high(n)
                elif kind == "out":
                    pick_out(n)
                else:
                    features_out(0, n)
            act.wait_ge(pads_ready, 2)
            act.wait_ge(picked_done, PICKS)
            nc.scalar.copy(features[:, :, PICKS], pick_ps[(PICKS - 1) % 2][:, 0, :]).then_inc(last_pick_put, 1)
            pick_out(PICKS - 1)
            pairs_out(0, True)
            act.wait_ge(mlp_in, 48)
            act.wait_ge(y_ready, 1)

            def tile_over_mlp(t):
                features_out(t, 1)
                h1_out(t - 1, 0)
                h1_out(t - 1, 1)
                features_out(t, 3)
                h2_out(t - 1, 0)
                for g in range(5, NT, 2):
                    features_out(t, g)
                h2_out(t - 1, 1)
                pairs_out(t, False)

            with act.Fori(1, TILES) as t:
                tile_over_mlp(t)
            t = TILES - 1
            h1_out(t, 0)
            h1_out(t, 1)
            h2_out(t, 0)
            h2_out(t, 1)
            y_out(t)

        @block.tensor
        def _(pe):
            def pick(i):
                if i == 0:
                    pe.wait_ge(first_hi_ready, 1)
                else:
                    pe.wait_ge(hi_ready, i + 1)
                if i >= 2:
                    pe.wait_ge(picks_ready, i - 1)
                acc = pick_ps[i % 2][:].rearrange("p a b -> p (a b)")
                for n, c in enumerate(PLACES):
                    if i == 0 and n == HALF:
                        pe.wait_ge(hi_ready, 1)
                    if c < ACT_RPP:
                        pe.wait_ge(onehot_act, ACT_RPP * i + c + 1)
                    else:
                        pe.wait_ge(onehot_ready, (RPP - ACT_RPP) * i + n + 1)
                    nc.tensor.matmul(acc, table_hi[i % 2][:, c, :], onehot[i % 2][:, c, :],
                                     start=(n == 0), stop=False)
                if i == 0:
                    pe.wait_ge(first_lo_ready, 1)
                else:
                    pe.wait_ge(lo_ready, i + 1)
                for n, c in enumerate(PLACES):
                    if i == 0 and n == HALF:
                        pe.wait_ge(lo_ready, 1)
                    last = nc.tensor.matmul(acc, table_lo[i % 2][:, c, :], onehot[i % 2][:, c, :],
                                            start=False, stop=(n == RPP - 1))
                last.then_inc(picked_done, 1)

            def turn(t, g):
                pe.wait_ge(rows_in[g], 16 * len(TURNS[g]) * (t + 1))
                if g >= 2:
                    if g % 2 == 0:
                        pe.wait_ge(feat_dve, EVEN * t + g // 2)
                    else:
                        pe.wait_ge(feat_act, ODD * t + g // 2)
                for i, slot in enumerate(TURNS[g]):
                    last = nc.tensor.transpose(turn_ps[g % 2][:, i, :], rows[:, slot - FIRST_G, :], ident[:])
                last.then_inc(turned, 1)

            def products(t, first):
                pe.wait_ge(static_put, t + 1)
                pe.wait_ge(feat_dve, EVEN * (t + 1))
                pe.wait_ge(feat_act, ODD * (t + 1))
                for k in range(BATCHES):
                    if not (first and k < 2):
                        pe.wait_ge(pairs_dve, BATCHES * t + k - 1)
                        pe.wait_ge(pairs_act, BATCHES * t + k - 1)
                    for m in range(BGROUPS):
                        b = (k * BGROUPS + m) * SPG
                        last = nc.tensor.matmul(
                            prod_ps[k % 2][0:FIRSTS, m, 0:SPG * COLS],
                            features[:, b:b + SPG, :].rearrange("p b f -> p (b f)")[:, 0:FIRSTS],
                            features[:, b:b + SPG, 1:FEATURES], start=True, stop=True)
                    last.then_inc(prods_done, 1)
                    if k == 0 and not first:
                        layer3(t - 1)

            def layer1_units(t, n, c, start, stop):
                k = LAST_ROWS if c == CHUNKS - 1 else 128
                rhs = static_t[:, 0, bass.ts(t, TILE)] if c == CHUNKS else pairs[0:k, c, :]
                return nc.tensor.matmul(mlp_ps[n // 2][:, n % 2, :], w1_sb[0:k, c, 128 * n:128 * n + 128], rhs,
                                        start=start, stop=stop, skip_group_check=True)

            def layer1(t, free):
                for n in (2, 3, 0, 1):
                    if n == 0:
                        pe.wait_ge(y_ready, free)
                    layer1_units(t, n, CHUNKS, n % 2 == 0, False)
                pe.wait_ge(pairs_dve, BATCHES * (t + 1))
                pe.wait_ge(pairs_act, BATCHES * (t + 1))
                for n in range(4):
                    for c in range(CHUNKS):
                        last = layer1_units(t, n, c, False, c == CHUNKS - 1)
                    if n % 2 == 1:
                        last.then_inc(h1_done, 1)

            def layer2(t, m):
                for c in range(4):
                    if m == 0 and c % 2 == 0:
                        pe.wait_ge(h1_ready, 2 * t + c // 2 + 1)
                    last = nc.tensor.matmul(mlp_ps[m][:, 2, :], w2_sb[:, c, 128 * m:128 * m + 128], h1[:, c, :],
                                            start=(c == 0), stop=(c == 3))
                last.then_inc(h2_done, 1)

            def layer3(t):
                for m in range(2):
                    pe.wait_ge(h2_ready, 2 * t + m + 1)
                    last = nc.tensor.matmul(mlp_ps[0][0:1, 3, :], w3_sb[:, m:m + 1], h2[:, m, :],
                                            start=(m == 0), stop=(m == 1))
                last.then_inc(y_done, 1)

            pe.wait_ge(warm_ready, 1)
            for _ in range(WARM_UP):
                nc.tensor.matmul(prod_ps[0][:, 0, :], h1[:, 0, :], h1[:, 0, :], start=True, stop=True)
            for kind, n in OPENING_PE:
                if kind == "pick":
                    pick(n)
                elif kind == "bottom":
                    pe.wait_ge(ident_ready, 1)
                    pe.wait_ge(bottom_in, 16)
                    for t in range(TILES):
                        last = nc.tensor.transpose(turn_ps[1][:, t, :], bottom_rows[:, t, :], ident[:])
                    last.then_inc(bottom_turned, 1)
                else:
                    if n == 1:
                        pe.wait_ge(bottom_ready, 1)
                    turn(0, n)
            pe.wait_ge(pads_ready, 2)
            pe.wait_ge(last_pick_put, 1)
            products(0, True)
            pe.wait_ge(w1_in, 16 * (CHUNKS + 1))
            pe.wait_ge(mlp_in, 48)

            def tile_over_mlp(t):
                turn(t, 0)
                turn(t, 1)
                layer1(t - 1, t)
                turn(t, 2)
                turn(t, 3)
                layer2(t - 1, 0)
                for g in range(4, NT):
                    turn(t, g)
                layer2(t - 1, 1)
                products(t, False)

            with pe.Fori(1, TILES) as t:
                tile_over_mlp(t)
            layer1(TILES - 1, TILES)
            layer2(TILES - 1, 0)
            layer2(TILES - 1, 1)
            layer3(TILES - 1)


_GATHERED = [f"tbl_{f}" for f in GATHERED]


def kernel(**inputs):
    import numpy as _np
    import concourse.bacc as _bacc
    from concourse import mybir as _mybir
    from concourse.bass_utils import run_bass_kernel_spmd as _run

    arrays = {n: _np.ascontiguousarray(inputs[n]) for n in ["r_bottom_output", "W_top2"] + _GATHERED}
    for n in ("b_top2", "W_top3"):
        arrays[n] = _np.ascontiguousarray(_np.asarray(inputs[n]).reshape(HID2 // 128, 128).T)
    ids = _np.asarray(inputs["ids"])
    arrays["picked_ids"] = _np.ascontiguousarray(ids[:, PICKED].T)
    picked = _np.zeros((PICKS, 128 * RPP, DIM), _np.float32)
    for i, f in enumerate(PICKED):
        picked[i, :PICK_ROWS] = _np.asarray(inputs[f"tbl_{f}"])
    arrays["picked"] = picked.reshape(PICKS, 128, RPP, DIM)
    arrays["ids"] = _np.ascontiguousarray(ids.reshape(TILES, TILE, TABLES).transpose(1, 0, 2))
    w = _np.asarray(inputs["W_top1"])
    w1 = _np.zeros(((CHUNKS + 1) * 128, HID1), w.dtype)
    pair_row = _np.zeros((FEATURES, FEATURES), _np.int64)
    first, second = _np.triu_indices(FEATURES, k=1)
    pair_row[first, second] = pair_row[second, first] = _np.arange(len(first))
    feature = _np.array([0] + [1 + f for f in ORDER])
    w1[128 * ((second - 1) // STRIPS) + 32 * ((second - 1) % STRIPS) + first] = \
        w[pair_row[feature[first], feature[second]]]
    w1[128 * (CHUNKS - 1) + 64] = _np.asarray(inputs["b_top1"])
    w1[128 * CHUNKS:] = w[len(first):]
    arrays["W_top1"] = w1

    nc = _bacc.Bacc("TRN2", target_bir_lowering=False, num_devices=1)
    ap = {n: nc.dram_tensor(f"in_{n}_dram", a.shape, _mybir.dt.from_np(a.dtype), kind="ExternalInput").ap()
          for n, a in arrays.items()}
    out = nc.dram_tensor("out_0_dram", (BATCH, 1), _mybir.dt.float32, kind="ExternalOutput").ap()
    dlrm_tower(nc, ap["r_bottom_output"], ap["ids"], ap["picked_ids"], ap["picked"],
               {f: ap[f"tbl_{f}"] for f in GATHERED}, ap["W_top1"], ap["W_top2"],
               ap["b_top2"], ap["W_top3"], out)
    r = _run(nc, [{f"in_{n}_dram": a for n, a in arrays.items()}], core_ids=[0])
    return r.results[0]["out_0_dram"]
```
